# Optimizing a Trainium2 kernel written in Bass

```python
import numpy as np
import jax
import jax.numpy as jnp

def _softmax(x, axis=-1):
    return jax.nn.softmax(x, axis=axis)

def _gelu(x):
    return jax.nn.gelu(x, approximate=True)

def _silu(x):
    return jax.nn.silu(x)

def _sigmoid(x):
    return jax.nn.sigmoid(x)

def _layernorm(x, axis=-1, eps=1e-05):
    m = jnp.mean(x, axis=axis, keepdims=True)
    v = jnp.var(x, axis=axis, keepdims=True)
    return (x - m) / jnp.sqrt(v + eps)

def _scatter_add(tgt, idx, src, axis=0):
    return tgt.at[idx].add(src)

def _segment_sum(src, seg, n):
    return jax.ops.segment_sum(src, seg, n)
kernel_name = 'mk_gnn_ffn_d2_gnn_r32_72069a'

def setup_inputs(seed: int=0):
    np.random.seed(seed)
    _w = jnp.asarray

    def _rec_inputs():
        import jax
        import jax.numpy as jnp
        _gk = jax.random.key(seed)
        x = -0.0003713 + 1 * jax.random.normal(jax.random.fold_in(_gk, 1), (3125, 256), jnp.float32)
        src = jax.random.randint(jax.random.fold_in(_gk, 2), (50000,), 0, 3125, jnp.int32)
        dst = jnp.minimum((3125 * jax.random.uniform(jax.random.fold_in(_gk, 3), (50000,)) ** 2.0).astype(jnp.int32), 99999)
        _o = jnp.argsort(dst, stable=True)
        src = src[_o]
        dst = dst[_o]
        return (x, src, dst)
    x, src, dst = _rec_inputs()

    def _L0_gnn_setup():
        import jax, jax.numpy as jnp
        import numpy as np
        N = 50000
        E = 25000
        IN, HID, OUT = (256, 512, 256)
        key = jax.random.key(seed)
        ks = jax.random.split(key, 8)
        x = jax.random.normal(ks[0], (N, IN), dtype=jnp.float32)
        edge_index = jax.random.randint(ks[1], (2, E), 0, N, dtype=jnp.int64)

        def lin(k, fan_out, fan_in):
            s = 1.0 / np.sqrt(fan_in)
            return jax.random.uniform(k, (fan_out, fan_in), jnp.float32, -s, s)
        return {'x': x, 'edge_index': edge_index, 'W1l': lin(ks[2], HID, IN), 'b1': jnp.zeros((HID,), jnp.float32), 'W1r': lin(ks[3], HID, IN), 'W2l': lin(ks[4], OUT, HID), 'b2': jnp.zeros((OUT,), jnp.float32), 'W2r': lin(ks[5], OUT, HID)}
    _L0_gnn_all = _L0_gnn_setup()
    _L0_gnn_in = {k: v for k, v in _L0_gnn_all.items() if k in ('W1l', 'b1', 'W1r', 'W2l', 'b2', 'W2r')}
    del _L0_gnn_all

    def _L0_ffn_setup():
        import jax, jax.numpy as jnp
        import numpy as np
        B, S, D, E, H, K = (4, 128, 256, 8, 512, 2)
        key = jax.random.key(seed)
        ks = jax.random.split(key, 6)
        x = jax.random.normal(ks[0], (B, S, D), jnp.float32)
        Wg = jax.random.normal(ks[1], (D, E), jnp.float32) * 0.02
        bg = jnp.zeros((E,), jnp.float32)
        W1 = jax.random.normal(ks[2], (E, D, H), jnp.float32) * 0.02
        b1 = jnp.zeros((E, H), jnp.float32)
        W2 = jax.random.normal(ks[3], (E, H, D), jnp.float32) * 0.02
        b2 = jnp.zeros((E, D), jnp.float32)
        return {'x': x, 'Wg': Wg, 'bg': bg, 'W1': W1, 'b1': b1, 'W2': W2, 'b2': b2}
    _L0_ffn_all = _L0_ffn_setup()
    _L0_ffn_in = {k: v for k, v in _L0_ffn_all.items() if k in ('Wg', 'bg', 'W1', 'b1', 'W2', 'b2')}
    del _L0_ffn_all

    def _L1_gnn_setup():
        import jax, jax.numpy as jnp
        import numpy as np
        N_NODES = 50000
        N_EDGES = 25000
        D = 256
        N_LAYERS = 2

        def _gcn_conv(x, W, b, src, dst, n):
            h = x @ W
            loops = jnp.arange(n, dtype=src.dtype)
            s = jnp.concatenate([src, loops])
            d = jnp.concatenate([dst, loops])
            deg = jax.ops.segment_sum(jnp.ones(s.shape[0], dtype=x.dtype), d, num_segments=n)
            dinv = jnp.where(deg > 0, deg ** (-0.5), 0.0)
            norm = dinv[s] * dinv[d]
            msg = h[s] * norm[:, None]
            return jax.ops.segment_sum(msg, d, num_segments=n) + b
        key = jax.random.key(seed)
        k1, k2, k3, k4, k5, k6 = jax.random.split(key, 6)
        inp = {}
        inp['input'] = jax.random.normal(k1, (N_NODES, D), dtype=jnp.float32)
        inp['edge_index'] = jax.random.randint(k2, (2, N_EDGES), 0, N_NODES, dtype=jnp.int64)
        scale = 1.0 / np.sqrt(D)
        inp['weight'] = jax.random.normal(k3, (D, D), dtype=jnp.float32) * scale
        inp['bias'] = jnp.zeros((D,), dtype=jnp.float32)
        inp['conv_w'] = jax.random.normal(k4, (N_LAYERS, D, D), dtype=jnp.float32) * scale
        inp['conv_b'] = jnp.zeros((N_LAYERS, D), dtype=jnp.float32)
        return inp
    _L1_gnn_all = _L1_gnn_setup()
    _L1_gnn_in = {k: v for k, v in _L1_gnn_all.items() if k in ('weight', 'bias', 'conv_w', 'conv_b')}
    del _L1_gnn_all

    def _L1_ffn_setup():
        import jax, jax.numpy as jnp
        import numpy as np
        B, T, D, H, E = (16, 128, 256, 512, 8)
        key = jax.random.key(seed)
        ks = jax.random.split(key, 5)
        x = jax.random.normal(ks[0], (B, T, D), dtype=jnp.float32)
        gate_w = jax.random.normal(ks[1], (D, E), dtype=jnp.float32) * 0.02
        gate_b = jnp.zeros((E,), dtype=jnp.float32)
        W1 = jax.random.normal(ks[2], (E, D, H), dtype=jnp.float32) * 0.02
        b1 = jnp.zeros((E, H), dtype=jnp.float32)
        W2 = jax.random.normal(ks[3], (E, H, D), dtype=jnp.float32) * 0.02
        b2 = jnp.zeros((E, D), dtype=jnp.float32)
        return {'x': x, 'gate_w': gate_w, 'gate_b': gate_b, 'W1': W1, 'b1': b1, 'W2': W2, 'b2': b2}
    _L1_ffn_all = _L1_ffn_setup()
    _L1_ffn_in = {k: v for k, v in _L1_ffn_all.items() if k in ('gate_w', 'gate_b', 'W1', 'b1', 'W2', 'b2')}
    del _L1_ffn_all
    return {'x': x, 'src': src, 'dst': dst, 'L0_gnn_W1l': _L0_gnn_in['W1l'], 'L0_gnn_b1': _L0_gnn_in['b1'], 'L0_gnn_W1r': _L0_gnn_in['W1r'], 'L0_gnn_W2l': _L0_gnn_in['W2l'], 'L0_gnn_b2': _L0_gnn_in['b2'], 'L0_gnn_W2r': _L0_gnn_in['W2r'], 'L0_ffn_Wg': _L0_ffn_in['Wg'], 'L0_ffn_bg': _L0_ffn_in['bg'], 'L0_ffn_W1': _L0_ffn_in['W1'], 'L0_ffn_b1': _L0_ffn_in['b1'], 'L0_ffn_W2': _L0_ffn_in['W2'], 'L0_ffn_b2': _L0_ffn_in['b2'], 'L1_gnn_weight': _L1_gnn_in['weight'], 'L1_gnn_bias': _L1_gnn_in['bias'], 'L1_gnn_conv_w': _L1_gnn_in['conv_w'], 'L1_gnn_conv_b': _L1_gnn_in['conv_b'], 'L1_ffn_gate_w': _L1_ffn_in['gate_w'], 'L1_ffn_gate_b': _L1_ffn_in['gate_b'], 'L1_ffn_W1': _L1_ffn_in['W1'], 'L1_ffn_b1': _L1_ffn_in['b1'], 'L1_ffn_W2': _L1_ffn_in['W2'], 'L1_ffn_b2': _L1_ffn_in['b2']}

def reference(x, src, dst, L0_gnn_W1l, L0_gnn_b1, L0_gnn_W1r, L0_gnn_W2l, L0_gnn_b2, L0_gnn_W2r, L0_ffn_Wg, L0_ffn_bg, L0_ffn_W1, L0_ffn_b1, L0_ffn_W2, L0_ffn_b2, L1_gnn_weight, L1_gnn_bias, L1_gnn_conv_w, L1_gnn_conv_b, L1_ffn_gate_w, L1_ffn_gate_b, L1_ffn_W1, L1_ffn_b1, L1_ffn_W2, L1_ffn_b2):
    import jax
    import jax.numpy as jnp

    def _L0_gnn_ref(x, edge_index, W1l, b1, W1r, W2l, b2, W2r):
        import jax, jax.numpy as jnp
        import numpy as np
        N = 50000
        E = 25000
        IN, HID, OUT = (256, 512, 256)
        src, dst = (edge_index[0], edge_index[1])
        n = x.shape[0]
        deg = jax.ops.segment_sum(jnp.ones((src.shape[0],), x.dtype), dst, num_segments=n)
        inv_deg = 1.0 / jnp.maximum(deg, 1.0)

        def sage(h, Wl, b, Wr):
            agg = jax.ops.segment_sum(h[src], dst, num_segments=n) * inv_deg[:, None]
            return agg @ Wl.T + b + h @ Wr.T
        h = jax.nn.relu(sage(x, W1l, b1, W1r))
        z = sage(h, W2l, b2, W2r)
        return z

    def _L0_ffn_ref(x, Wg, bg, W1, b1, W2, b2):
        import jax, jax.numpy as jnp
        import numpy as np
        B, S, D, E, H, K = (4, 128, 256, 8, 512, 2)
        Bv, Sv, Dv = x.shape
        gate_scores = x @ Wg + bg
        _, idx = jax.lax.top_k(gate_scores, K)
        mask = jax.nn.one_hot(idx, E, dtype=x.dtype).sum(axis=-2)
        xf = x.reshape(-1, Dv)
        mf = mask.reshape(-1, E)
        h = jax.nn.gelu(jnp.einsum('td,edh->teh', xf, W1) + b1[None], approximate=False)
        y = jnp.einsum('teh,ehd->ted', h, W2) + b2[None]
        out = jnp.einsum('ted,te->td', y, mf)
        return out.reshape(Bv, Sv, Dv)

    def _L1_gnn_ref(input, edge_index, weight, bias, conv_w, conv_b):
        import jax, jax.numpy as jnp
        import numpy as np
        N_NODES = 50000
        N_EDGES = 25000
        D = 256
        N_LAYERS = 2

        def _gcn_conv(x, W, b, src, dst, n):
            h = x @ W
            loops = jnp.arange(n, dtype=src.dtype)
            s = jnp.concatenate([src, loops])
            d = jnp.concatenate([dst, loops])
            deg = jax.ops.segment_sum(jnp.ones(s.shape[0], dtype=x.dtype), d, num_segments=n)
            dinv = jnp.where(deg > 0, deg ** (-0.5), 0.0)
            norm = dinv[s] * dinv[d]
            msg = h[s] * norm[:, None]
            return jax.ops.segment_sum(msg, d, num_segments=n) + b
        n = input.shape[0]
        src, dst = (edge_index[0], edge_index[1])
        x = jax.nn.relu(input @ weight + bias)
        for i in range(conv_w.shape[0]):
            x = jax.nn.relu(_gcn_conv(x, conv_w[i], conv_b[i], src, dst, n))
        return x

    def _L1_ffn_ref(x, gate_w, gate_b, W1, b1, W2, b2):
        import jax, jax.numpy as jnp
        import numpy as np
        B, T, D, H, E = (16, 128, 256, 512, 8)
        Bb, Tt, Dd = x.shape
        Ee = gate_w.shape[1]
        xf = x.reshape(-1, Dd)
        N = xf.shape[0]
        logits = xf @ gate_w + gate_b
        probs = jax.nn.softmax(logits, axis=-1)
        top2_vals, top2_idx = jax.lax.top_k(probs, 2)
        cw = jnp.zeros((N, Ee), dtype=xf.dtype).at[jnp.arange(N)[:, None], top2_idx].add(top2_vals)

        def step(acc, params):
            w1, bb1, w2, bb2, we = params
            h = jax.nn.gelu(xf @ w1 + bb1, approximate=False)
            y = h @ w2 + bb2
            return (acc + we[:, None] * y, None)
        out, _ = jax.lax.scan(step, jnp.zeros_like(xf), (W1, b1, W2, b2, cw.T))
        return out.reshape(Bb, Tt, Dd)
    edge_index = jnp.stack([src, dst])
    x = x + _L0_gnn_ref(_layernorm(x, axis=-1), edge_index, L0_gnn_W1l, L0_gnn_b1, L0_gnn_W1r, L0_gnn_W2l, L0_gnn_b2, L0_gnn_W2r)
    x = x + _L0_ffn_ref(_layernorm(x, axis=-1)[None], L0_ffn_Wg, L0_ffn_bg, L0_ffn_W1, L0_ffn_b1, L0_ffn_W2, L0_ffn_b2)[0]
    x = x + _L1_gnn_ref(_layernorm(x, axis=-1), edge_index, L1_gnn_weight, L1_gnn_bias, L1_gnn_conv_w, L1_gnn_conv_b)
    x = x + _L1_ffn_ref(_layernorm(x, axis=-1)[None], L1_ffn_gate_w, L1_ffn_gate_b, L1_ffn_W1, L1_ffn_b1, L1_ffn_W2, L1_ffn_b2)[0]
    return x

_drawn_inputs = setup_inputs


def setup_inputs(seed=0):
    import zlib

    import numpy as np

    out = dict(_drawn_inputs(seed))
    spreads = {'L0_gnn_b1': (0.0, 0.1),
     'L0_gnn_b2': (0.0, 0.1),
     'L0_ffn_bg': (0.0, 0.1),
     'L0_ffn_b1': (0.0, 0.1),
     'L0_ffn_b2': (0.0, 0.1),
     'L1_gnn_bias': (0.0, 0.351),
     'L1_gnn_conv_b': (0.0, 0.1),
     'L1_ffn_gate_b': (0.0, 0.608),
     'L1_ffn_b1': (0.0, 0.8),
     'L1_ffn_b2': (0.0, 0.352)}
    factors = {'L1_ffn_W1': 3.173, 'L1_ffn_W2': 2.934}
    for name, (base, spread) in spreads.items():
        noise = np.random.default_rng([zlib.crc32(name.encode()), seed]).standard_normal(out[name].shape)
        drawn = base * np.exp(spread * noise) if base else spread * noise
        out[name] = jnp.asarray(drawn.astype(out[name].dtype))
    for name, factor in factors.items():
        out[name] = (out[name] * factor).astype(out[name].dtype)
    return out
```

```python
from contextlib import ExitStack

import numpy as np
import concourse.bass as bass
from concourse import mybir
from concourse.bass import ds

F32 = mybir.dt.float32
F16 = mybir.dt.float16
I32 = mybir.dt.int32
ALU = mybir.AluOpType
ACT = mybir.ActivationFunctionType
AX = mybir.AxisListType
ABSMAX = bass.bass_isa.ReduceOp.absmax

P = 128
N_NODES = 3125
N_EDGES = 50000
D = 256
KB = D // P
TILES = -(-N_NODES // P)
NP = TILES * P
TAIL = N_NODES - (TILES - 1) * P
U = 5
GROUPS = TILES // U
CHUNK = U * P
HALF = CHUNK // 2
ETILES = -(-N_EDGES // P)
ECOLS = 512
EPAD_DST = 4096
WIN = 16
WPB = P // WIN
WINDOWS = NP // WIN
WCOLS = TILES * WIN
HID = 512
HB = HID // P
E = 8
SLOTS = 4
ATCOLS = TILES * P
XS = 256.0
EXPO = 0x7F800000
GNNW = 4096 + 1536 + 32


class Scratch:

    def __init__(self, ap):
        self.ap, self.at = ap, 0

    def take(self, n):
        self.at += n
        assert self.at <= self.ap.shape[1]
        return self.ap[:, self.at - n:self.at]


class Core:

    def __init__(self, nc, ctx, dram):
        self.nc, self.ctx, self.dram = nc, ctx, dram
        self.sems = []
        sb = self.sb
        self.X = sb("x_resid", [P, TILES * D], F32)
        self.XTh = sb("xT_hi", [P, KB * NP], F16)
        self.XTl = sb("xT_lo", [P, KB * NP], F16)
        self.HL = sb("rows_hi_lo", [P, TILES * 2 * D], F16)
        self.MTh = sb("mT_hi", [P, KB * NP], F16)
        self.MTl = sb("mT_lo", [P, KB * NP], F16)
        self.G = sb("rows_f32", [P, TILES * D], F32)
        self.ATB = sb("stream", [P, 16384], F16)
        self.G0W = sb("gnn0_w", [P, 2, 4096], F16)
        self.G1W = sb("gnn1_w", [P, 2, 1536 + 32], F16)
        self.HF = sb("hidden_f32", [P, 2, CHUNK], F32)
        self.ident = sb("ident", [P, P], F32)
        self.R = sb("row_slots", [P, U, D], F32)
        self.TMP = sb("lo_slots", [P, U, D], F32)
        self.ROWB = sb("row_bias", [P, 3, D], F32)
        self.COLB = sb("col_bias", [P, HB + KB], F32)
        self.GATEB = sb("gate_bias", [P, 2, E], F32)
        self.FB1 = sb("ffn_b1", [P, 2, E * HB], F32)
        self.FB2 = sb("ffn_b2", [E, 2, D], F32)
        self.INV = sb("inv_deg", [P, TILES], F32)
        self.DINV = sb("deg_rsqrt", [P, TILES], F32)
        self.SCL = sb("agg_scale", [P, TILES], F32)
        self.EPSP = sb("minus_half", [P, TILES], F32)
        self.MX = sb("maxima", [P, 12], F32)
        self.MXR = sb("maxima_all", [P, 12], F32)
        self.SIG = sb("scale_up", [P, 12], F32)
        self.PK = sb("scale_down", [P, 12], F32)
        self.SG = sb("gate_scores", [P, TILES * E], F32)
        self.CW = sb("gate_weights", [P, TILES * E], F32)
        self.CWK = sb("gate_weights_scaled", [P, E * TILES], F32)
        self.ST = sb("row_stats", [P, TILES * 6], F32)
        self.STV = sb("row_moments", [P, 4, TILES], F32)
        self.ELOW = sb("expert_below", [P, E * E], F32)
        self.EK = sb("expert_factors", [P, 3, E], F32)
        self.EM = sb("expert_max", [P, 3], F32)
        self.EMR = sb("expert_max_all", [P, 3], F32)
        self.ESIG = sb("expert_up", [P, 3], F32)
        self.EPK = sb("expert_down", [P, 3], F32)
        self.FAC = sb("out_factors", [P, 2 + TILES], F32)
        self.DEG = sb("degree", [P, TILES], F32)
        self.DTMP = sb("degree_at_least_1", [P, TILES], F32)
        early = Scratch(self.MTh[:].bitcast(F32))
        self.KEY, self.CMB = early.take(ECOLS), early.take(ECOLS)
        self.IOTA, self.WNEG, self.EDIFF = early.take(WCOLS), early.take(WINDOWS), early.take(E * E)
        self.IOTAH, self.ZERO = early.take(WCOLS // 2).bitcast(F16), early.take(P // 2).bitcast(F16)
        self.ONE = early.take(1).bitcast(F16)[:, 0:1]
        self.MROW = self.MTl[:].bitcast(I32)[0:1, 0:2 * P]
        early = Scratch(self.MTl[:].bitcast(F32)[:, 4 * P:])
        self.OHK, self.OHC = early.take(SLOTS * P // 2).bitcast(F16), early.take(SLOTS * WCOLS // 2).bitcast(F16)
        self.CMP = self.MTh[:].bitcast(F32).rearrange("p (n w) -> p n w", n=2)
        late = Scratch(self.MTl[:].bitcast(F32))
        self.RANK, self.MEX = late.take(TILES * E), late.take(TILES)
        self.CWR = late.take(U * E).rearrange("p (u e) -> p u e", u=U)
        self.CWT = late.take(U * P)[0:E, :].rearrange("p (u n) -> p u n", u=U)
        self.PS = ctx.enter_context(nc.psum_tensor("psum", [P, 8, 512], F32))

    def sb(self, name, shape, dt):
        return self.ctx.enter_context(self.nc.sbuf_tensor(name, shape, dt))

    def sem(self, name):
        self.sems.append(self.nc.alloc_semaphore(name=name))
        return self.sems[-1]

    def clear_semaphores(self):
        self.nc.all_engine_barrier()
        self.nc.clear_and_free_semaphores(self.sems)
        self.nc.all_engine_barrier()
        self.sems = []

    def rows(self, t, j):
        return t[:, ds(j * D, D)]

    def cols(self, t, j):
        return t[:].rearrange("p (k n) -> p k n", k=KB)[:, :, ds(j * P, P)]


def setup_phase(c):
    nc, dram = c.nc, c.dram
    stage = c.ATB[:].bitcast(F32)
    words = Scratch(c.G[:])
    more = Scratch(c.HL[:].bitcast(F32))
    src, dst, ia, ib = (words.take(4 * P).bitcast(I32).rearrange("p (c e) -> p c e", c=4) for _ in range(4))
    keyf, cmbf, dwf = (words.take(4 * P).rearrange("p (c e) -> p c e", c=4) for _ in range(3))
    diag = words.take(8 * P).rearrange("p (c e) -> p c e", c=8)
    ones, tidx = words.take(P), words.take(ECOLS)
    inr, fv, ev = (more.take(2 * ECOLS).rearrange("p (g t) -> p g t", g=2) for _ in range(3))
    tmm = more.take(8).rearrange("p (m c) -> p m c", m=2)
    widx = more.take(2)
    wst = more.take(16).rearrange("p (k g) -> p k g", g=2)
    wint = more.take(2).bitcast(I32)
    KEY, CMB, MROW = c.KEY, c.CMB, c.MROW
    ld_x, ld_e, ld_w, ld_b = c.sem("x_loaded"), c.sem("edges_loaded"), c.sem("weights_loaded"), c.sem("biases_loaded")
    zeroed, consts = c.sem("zeroed"), c.sem("constants")
    dve, pool, pe = c.sem("setup_dve"), c.sem("setup_pool"), c.sem("setup_pe")
    meta_out, meta_in = c.sem("meta_stored"), c.sem("meta_loaded")

    with nc.Block() as block:
        @block.sync
        def _(sp):
            sp.wait_ge(zeroed, 3)
            full = (TILES - 1) * P
            for n, (t, name) in enumerate(((src, "src"), (dst, "dst"))):
                a = dram[name]
                sp.dma_start(t[:, 0:3, :], a[0:3 * P * P].rearrange("(c r e) -> r c e", c=3, r=P)).then_inc(ld_e, 16)
                at, whole = 3 * P * P, (N_EDGES - 3 * P * P) // P
                sp.dma_start(t[0:whole, 3, :], a[at:at + whole * P].rearrange("(r e) -> r e", e=P)).then_inc(ld_e, 16)
                at += whole * P
                sp.dma_start(t[whole:whole + 1, 3, 0:N_EDGES - at], a[at:].rearrange("(r e) -> r e", r=1)).then_inc(ld_e, 16)
            x3 = c.X[:].rearrange("p (t d) -> p t d", d=D)
            sp.dma_start(x3[:, 0:TILES - 1, :], dram["x"][0:full].rearrange("(t p) d -> p t d", p=P)).then_inc(ld_x, 16)
            sp.dma_start(x3[0:TAIL, TILES - 1, :], dram["x"][full:]).then_inc(ld_x, 16)
            sp.dma_start(stage[:, 0:GNNW], dram["gnn_w"]).then_inc(ld_w, 16)
            sp.dma_start(c.COLB[:], dram["col_bias"]).then_inc(ld_b, 16)
            for n, name in enumerate(("L0_gnn_b2", "conv_b0", "conv_b1")):
                sp.dma_start(c.ROWB[:, n, :], dram[name].partition_broadcast(P)).then_inc(ld_b, 16)
            for n, name in enumerate(("L0_ffn_bg", "L1_ffn_gate_b")):
                sp.dma_start(c.GATEB[:, n, :], dram[name].partition_broadcast(P)).then_inc(ld_b, 16)
            sp.dma_start(c.FB1[:], dram["ffn_b1"]).then_inc(ld_b, 16)
            for n, name in enumerate(("L0_ffn_b2", "L1_ffn_b2")):
                sp.dma_start(c.FB2[:, n, :], dram[name]).then_inc(ld_b, 16)
            sp.wait_ge(ld_x, 32)
            sp.wait_ge(dve, SETUP_META)
            sp.dma_start(dram["meta"].rearrange("(g p) -> p g", p=P), wint, allow_slow_non_contiguous=True).then_inc(meta_out, 16)
            sp.wait_ge(meta_out, 16)
            sp.dma_start(MROW, dram["meta"].rearrange("(a w) -> a w", a=1)).then_inc(meta_in, 16)
            sp.wait_ge(meta_in, 16)

        @block.gpsimd
        def _(pool_e):
            g = nc.gpsimd
            g.memset(c.ident[:], 0.0).then_inc(consts, 1)
            g.memset(ones[:], 1.0).then_inc(consts, 1)
            g.memset(c.EPSP[:], -0.5).then_inc(consts, 1)
            g.iota(c.IOTA[:], [[1, WCOLS]], base=0, channel_multiplier=0, allow_small_or_imprecise_dtypes=True).then_inc(consts, 1)
            g.iota(tidx[:], [[1, ECOLS]], base=0, channel_multiplier=0, allow_small_or_imprecise_dtypes=True).then_inc(consts, 1)
            g.iota(widx[:], [[P, 2]], base=0, channel_multiplier=1, allow_small_or_imprecise_dtypes=True).then_inc(consts, 1)
            g.iota(c.WNEG[:], [[-P, WINDOWS]], base=0, channel_multiplier=0, allow_small_or_imprecise_dtypes=True).then_inc(consts, 1)
            g.iota(c.EDIFF[:], [[1, E], [-1, E]], base=0, channel_multiplier=0, allow_small_or_imprecise_dtypes=True).then_inc(consts, 1)
            pool_e.wait_ge(consts, 8)
            g.affine_select(out=c.ident[:], in_=c.ident[:], compare_op=ALU.not_equal, fill=1.0, base=0,
                            pattern=[[-1, P]], channel_multiplier=1).then_inc(consts, 1)
            pool_e.wait_ge(dve, SETUP_MAX)
            g.partition_all_reduce(c.MXR[:, 0:9], c.MX[:, 0:9], P, ABSMAX).then_inc(pool, 1)

        @block.vector
        def _(v):
            n = [0]

            def step(ins):
                n[0] += 1
                ins.then_inc(dve, 1)

            nc.vector.memset(c.X[:, (TILES - 1) * D:], 0.0).then_inc(zeroed, 1)
            nc.vector.memset(src[:, 3, :], 0).then_inc(zeroed, 1)
            nc.vector.memset(dst[:, 3, :], EPAD_DST).then_inc(zeroed, 1)
            v.wait_ge(ld_w, 16)
            v.wait_ge(ld_b, 16 * 9)
            cuts = [(0, 2048), (2048, 4096), (4096, 4608), (4608, 5120), (5120, 5632), (5632, 5648), (5648, 5664)]
            for k, (a, b) in enumerate(cuts):
                step(nc.vector.tensor_reduce(c.MX[:, k:k + 1], stage[:, a:b], AX.X, ALU.max, apply_absolute_value=True))
            step(nc.vector.tensor_reduce(c.MX[:, 7:8], c.COLB[:, 0:HB], AX.X, ALU.max, apply_absolute_value=True))
            step(nc.vector.tensor_reduce(c.MX[:, 8:9], c.COLB[:, HB:HB + KB], AX.X, ALU.max, apply_absolute_value=True))
            assert n[0] == SETUP_MAX
            v.wait_ge(ld_e, 16 * 6)
            v.wait_ge(consts, 9)
            step(nc.vector.tensor_scalar(ia[:], src[:], 7, 4, ALU.logical_shift_right, ALU.logical_shift_left))
            step(nc.vector.tensor_scalar(ib[:], dst[:], WIN - 1, None, ALU.bitwise_and))
            v.wait_ge(dve, n[0])
            step(nc.vector.tensor_tensor(ia[:], ia[:], ib[:], ALU.bitwise_or))
            v.wait_ge(dve, n[0])
            step(nc.vector.tensor_copy(cmbf[:], ia[:]))
            v.wait_ge(dve, n[0])
            step(nc.vector.tensor_scalar(ia[:], dst[:], 4, 7, ALU.logical_shift_right, ALU.logical_shift_left))
            step(nc.vector.tensor_scalar(ib[:], src[:], P - 1, None, ALU.bitwise_and))
            v.wait_ge(dve, n[0])
            step(nc.vector.tensor_tensor(ia[:], ia[:], ib[:], ALU.bitwise_or))
            v.wait_ge(dve, n[0])
            step(nc.vector.tensor_copy(keyf[:], ia[:]))
            step(nc.vector.tensor_scalar(ib[:], dst[:], 4, None, ALU.logical_shift_right))
            v.wait_ge(dve, n[0])
            step(nc.vector.tensor_copy(dwf[:], ib[:]))
            v.wait_ge(dve, n[0])
            step(nc.vector.tensor_reduce(tmm[:, 0, :], dwf[:], AX.X, ALU.min))
            step(nc.vector.tensor_reduce(tmm[:, 1, :], dwf[:], AX.X, ALU.max))
            v.wait_ge(dve, n[0])
            for k in range(8):
                step(nc.vector.tensor_scalar(diag[:, k, :], c.ident[:], tmm[:, k // 4, k % 4:k % 4 + 1], None, ALU.mult))
            assert n[0] == SETUP_DIAG
            v.wait_ge(pe, 3)
            step(nc.vector.tensor_copy(KEY[:], c.PS[:, 0, :]))
            step(nc.vector.tensor_copy(CMB[:], c.PS[:, 1, :]))
            for g in range(2):
                step(nc.vector.tensor_scalar(inr[:, g, :], c.PS[:, 2, :], widx[:, g:g + 1], None, ALU.is_le))
            v.wait_ge(dve, n[0])
            for g in range(2):
                step(nc.vector.scalar_tensor_tensor(inr[:, g, :], c.PS[:, 3, :], widx[:, g:g + 1], inr[:, g, :], ALU.is_ge, ALU.mult))
            v.wait_ge(dve, n[0])
            for g in range(2):
                step(nc.vector.scalar_tensor_tensor(fv[:, g, :], tidx[:], -float(ECOLS), inr[:, g, :], ALU.add, ALU.mult))
                step(nc.vector.scalar_tensor_tensor(ev[:, g, :], tidx[:], 1.0, inr[:, g, :], ALU.add, ALU.mult))
            v.wait_ge(dve, n[0])
            step(nc.vector.tensor_reduce(wst[:, 0, :], fv[:], AX.X, ALU.min))
            step(nc.vector.tensor_reduce(wst[:, 1, :], ev[:], AX.X, ALU.max))
            v.wait_ge(dve, n[0])
            step(nc.vector.tensor_scalar(wst[:, 2, :], wst[:, 0, :], float(ECOLS), None, ALU.add))
            step(nc.vector.tensor_scalar(wst[:, 3, :], wst[:, 1, :], 1.0, None, ALU.max))
            v.wait_ge(dve, n[0])
            step(nc.vector.scalar_tensor_tensor(wst[:, 4, :], wst[:, 3, :], -1.0, wst[:, 2, :], ALU.add, ALU.min))
            v.wait_ge(dve, n[0])
            step(nc.vector.tensor_tensor(wst[:, 5, :], wst[:, 3, :], wst[:, 4, :], ALU.subtract))
            v.wait_ge(dve, n[0])
            step(nc.vector.scalar_tensor_tensor(wst[:, 6, :], wst[:, 5, :], 1024.0, wst[:, 4, :], ALU.mult, ALU.add))
            v.wait_ge(dve, n[0])
            step(nc.vector.tensor_copy(wint, wst[:, 6, :]))
            assert n[0] == SETUP_META
            step(nc.vector.tensor_copy(c.IOTAH[:], c.IOTA[:]))
            step(nc.vector.memset(c.ZERO[:], 0.0))
            step(nc.vector.memset(c.ONE[:], 1.0))
            step(nc.vector.tensor_scalar(c.ELOW[:], c.EDIFF[:], 0.0, None, ALU.is_gt))
            v.wait_ge(pool, 1)
            step(nc.vector.tensor_copy(c.MX[:, 0:9], c.MXR[:, 0:9]))
            v.wait_ge(dve, n[0])
            step(nc.vector.scalar_tensor_tensor(c.MX[:, 9:10], c.MX[:, 0:1], 512.0, c.MX[:, 7:8], ALU.mult, ALU.add))
            step(nc.vector.scalar_tensor_tensor(c.MX[:, 10:11], c.MX[:, 2:3], 256.0, c.MX[:, 8:9], ALU.mult, ALU.add))
            v.wait_ge(dve, n[0])
            step(nc.vector.tensor_scalar(c.MX[:, 0:11], c.MX[:, 0:11], 1e-30, None, ALU.max))
            v.wait_ge(dve, n[0])
            step(nc.vector.tensor_scalar(c.SIG[:, 0:11].bitcast(I32), c.MX[:, 0:11].bitcast(I32), EXPO, EXPO, ALU.bitwise_and, ALU.bitwise_xor))
            step(nc.vector.tensor_scalar(c.PK[:, 0:11].bitcast(I32), c.MX[:, 0:11].bitcast(I32), EXPO, None, ALU.bitwise_and))
            v.wait_ge(dve, n[0])
            step(nc.vector.tensor_scalar(c.SIG[:, 0:9], c.SIG[:, 0:9], 512.0, None, ALU.mult))
            step(nc.vector.tensor_scalar(c.SIG[:, 9:11], c.SIG[:, 9:11], 8192.0, None, ALU.mult))
            v.wait_ge(dve, n[0])
            parts = [(c.G0W, a, b, a, k) for k, (a, b) in enumerate(cuts[:2])] + [(c.G1W, a, b, a - 4096, k + 2) for k, (a, b) in enumerate(cuts[2:])]
            for t, a, b, o, k in parts:
                step(nc.vector.tensor_scalar(t[:, 0, o:o + b - a], stage[:, a:b], c.SIG[:, k:k + 1], None, ALU.mult))
            v.wait_ge(dve, n[0])
            for t, a, b, o, k in parts:
                step(nc.vector.scalar_tensor_tensor(t[:, 1, o:o + b - a], stage[:, a:b], c.SIG[:, k:k + 1], t[:, 0, o:o + b - a], ALU.mult, ALU.subtract))
            v.wait_ge(ld_x, 32)

        @block.tensor
        def _(t):
            t.wait_ge(dve, SETUP_DIAG)
            for k in range(4):
                m = nc.tensor.transpose(c.PS[:, 0, k * P:(k + 1) * P], keyf[:, k, :], c.ident[:])
            m.then_inc(pe, 1)
            for k in range(4):
                m = nc.tensor.transpose(c.PS[:, 1, k * P:(k + 1) * P], cmbf[:, k, :], c.ident[:])
            m.then_inc(pe, 1)
            for k in range(8):
                m = nc.tensor.matmul(c.PS[:, 2 + k // 4, k % 4 * P:(k % 4 + 1) * P], ones, diag[:, k, :], start=True, stop=True)
            m.then_inc(pe, 1)


SETUP_MAX = 9
SETUP_DIAG = SETUP_MAX + 12 + 8
SETUP_META = SETUP_DIAG + 2 + 2 + 2 + 4 + 2 + 2 + 1 + 1 + 1 + 1


class Windows:

    def __init__(self, c, eng, tag):
        self.c, self.eng = c, eng
        self.ranges = [eng.alloc_register(f"{tag}_range{k}") for k in range(WPB)]
        self.tile, self.count, self.visited = (eng.alloc_register(f"{tag}_{x}") for x in ("tile", "count", "visited"))
        eng.reg_mov(self.visited, 0)

    def load(self, b):
        self.eng.load(self.ranges, self.c.MROW[0:1, ds(b * WPB, WPB)])

    def tiles(self, k):
        self.eng.reg_alu(self.tile, self.ranges[k], 1023, ALU.bitwise_and)
        self.eng.reg_alu(self.count, self.ranges[k], 10, ALU.logical_shift_right)
        return self.eng.snap(self.count, min_val=1, max_val=ETILES)

    def here(self):
        tile = self.eng.snap(self.tile, min_val=0, max_val=ETILES - 1)
        visited = self.eng.snap(self.visited, min_val=0, max_val=WINDOWS * ETILES)
        return tile, visited, visited & (SLOTS - 1)

    def next(self):
        self.eng.reg_add(self.tile, self.tile, 1)
        self.eng.reg_add(self.visited, self.visited, 1)


def adjacency_phase(c):
    nc = c.nc
    OHK, OHC, DEG, DTMP = c.OHK, c.OHC, c.DEG, c.DTMP
    hot = c.sem("one_hots_ready")
    hot_used = c.sem("one_hots_used")
    win_full, win_free = c.sem("window_summed"), c.sem("window_copied")
    deg_full, deg_free = c.sem("degree_summed"), c.sem("degree_copied")
    stored = c.sem("block_stored")
    dv, pl = c.sem("degree_steps"), c.sem("degree_pow")

    with nc.Block() as block:
        @block.vector
        def _(v):
            walk = Windows(c, v, "dve")
            with v.Fori(0, TILES) as b:
                walk.load(b)
                for k in range(WPB):
                    wneg = c.WNEG[:, ds(b * WPB + k, 1)]
                    with v.Fori(0, walk.tiles(k)):
                        tile, visited, slot = walk.here()
                        v.wait_ge(hot_used, visited + 1)
                        nc.vector.tensor_scalar(OHC[:, ds(slot * WCOLS, WCOLS)], c.IOTAH[:], c.CMB[:, ds(tile, 1)], None, ALU.is_equal)
                        nc.vector.tensor_scalar(OHK[:, ds(slot * P, P)], c.IOTA[:, 0:P], c.KEY[:, ds(tile, 1)], wneg, ALU.subtract, ALU.is_equal).then_inc(hot, 1)
                        walk.next()
            v.wait_ge(deg_free, TILES + 1)
            nc.vector.tensor_scalar(DTMP[:], DEG[:], 1.0, None, ALU.max).then_inc(dv, 1)
            v.wait_ge(dv, 1)
            nc.vector.reciprocal(c.INV[:], DTMP[:]).then_inc(dv, 1)
            nc.vector.tensor_scalar(DEG[:], DEG[:], 1.0, None, ALU.add).then_inc(dv, 1)

        @block.tensor
        def _(t):
            t.sem_inc(hot_used, SLOTS)
            walk = Windows(c, t, "pe")
            with t.Fori(0, TILES) as b:
                walk.load(b)
                for k in range(WPB):
                    out = c.PS[:, k % 2, 0:WCOLS]
                    t.wait_ge(win_free, b * WPB + k + 1)
                    nc.tensor.matmul(out, c.ZERO[:], c.IOTAH[:], start=True, stop=False)
                    with t.Fori(0, walk.tiles(k)):
                        _, visited, slot = walk.here()
                        t.wait_ge(hot, visited + 1)
                        nc.tensor.matmul(out, OHK[:, ds(slot * P, P)], OHC[:, ds(slot * WCOLS, WCOLS)], start=False, stop=False).then_inc(hot_used, 1)
                        walk.next()
                    nc.tensor.matmul(out, c.ZERO[:], c.IOTAH[:], start=False, stop=True).then_inc(win_full, 1)
                t.wait_ge(win_free, b * WPB + WPB + 2)
                t.wait_ge(deg_free, b + 1)
                for s in range(TILES):
                    m = nc.tensor.matmul(c.PS[:, 2, 0:1], c.ATB[:, ds((b & 1) * ATCOLS + s * P, P)], c.ONE[:], start=(s == 0), stop=(s == TILES - 1))
                m.then_inc(deg_full, 1)

        @block.scalar
        def _(a):
            a.sem_inc(win_free, 2)
            a.sem_inc(deg_free, 1)
            with a.Fori(0, TILES) as b:
                for k in range(WPB):
                    a.wait_ge(win_full, b * WPB + k + 1)
                    half = c.ATB[:, ds((b & 1) * ATCOLS, ATCOLS)].rearrange("p (s d) -> p s d", d=P)
                    nc.scalar.copy(half[:, :, k * WIN:(k + 1) * WIN], c.PS[:, k % 2, 0:WCOLS].rearrange("p (s d) -> p s d", d=WIN)).then_inc(win_free, 1)
                a.wait_ge(deg_full, b + 1)
                nc.scalar.copy(DEG[:, ds(b, 1)], c.PS[:, 2, 0:1]).then_inc(deg_free, 1)
                a.wait_ge(stored, b * 16 + 1)

        @block.sync
        def _(sp):
            before, copied, row, half = (sp.alloc_register(f"store_{x}") for x in ("before", "copied", "row", "half"))
            sp.sem_inc(stored, 1)
            for register, first in ((before, 1), (copied, WPB + 2), (row, 0), (half, 0)):
                sp.reg_mov(register, first)
            with sp.Fori(0, TILES) as b:
                sp.wait_ge(stored, before)
                sp.wait_ge(win_free, copied)
                sp.dma_start(c.dram["adj"].rearrange("a p n -> (a p) n")[ds(sp.snap(row, min_val=0, max_val=(TILES - 1) * P), P)],
                             c.ATB[:, ds(sp.snap(half, min_val=0, max_val=ATCOLS), ATCOLS)]).then_inc(stored, 16)
                for register, add in ((before, 16), (copied, WPB), (row, P)):
                    sp.reg_add(register, register, add)
                sp.reg_alu(half, half, ATCOLS, ALU.bitwise_xor)
            sp.wait_ge(stored, TILES * 16 + 1)

        @block.gpsimd
        def _(g):
            g.wait_ge(dv, 3)
            nc.gpsimd.tensor_tensor(c.DINV[:], DEG[:], c.EPSP[:], ALU.pow).then_inc(pl, 1)


def turn(c, tag, source, dst_h, dst_l, nodes):
    nc = c.nc
    ST = c.ST
    V = c.STV
    stat, dv, pl = c.sem(f"{tag}_stats"), c.sem(f"{tag}_moments"), c.sem(f"{tag}_rsqrt")
    row, up, hi, lo = c.sem(f"{tag}_row"), c.sem(f"{tag}_turned"), c.sem(f"{tag}_hi"), c.sem(f"{tag}_lo")
    kept = c.sem(f"{tag}_kept")
    kept_hi = c.sem(f"{tag}_kept_hi")

    with nc.Block() as block:
        @block.vector
        def _(v):
            v.sem_inc(lo, U)
            if source == "norm":
                with v.Fori(0, TILES) as j:
                    nc.vector.bn_stats(ST[:, ds(j * 6, 6)], c.rows(c.X, j)).then_inc(stat, 1)
                v.wait_ge(stat, TILES)
                s = ST[:].rearrange("p (t s) -> p s t", s=6)
                nc.vector.tensor_tensor(V[:, 0, :], s[:, 1, :], s[:, 4, :], ALU.add).then_inc(dv, 1)
                nc.vector.tensor_tensor(V[:, 1, :], s[:, 1, :], s[:, 4, :], ALU.subtract).then_inc(dv, 1)
                nc.vector.tensor_tensor(V[:, 2, :], s[:, 2, :], s[:, 5, :], ALU.add).then_inc(dv, 1)
                v.wait_ge(dv, 3)
                nc.vector.tensor_scalar(V[:, 0, :], V[:, 0, :], 0.5, None, ALU.mult).then_inc(dv, 1)
                nc.vector.tensor_tensor(V[:, 1, :], V[:, 1, :], V[:, 1, :], ALU.mult).then_inc(dv, 1)
                nc.vector.tensor_scalar(V[:, 2, :], V[:, 2, :], 1.0 / D, 1e-5, ALU.mult, ALU.add).then_inc(dv, 1)
                v.wait_ge(dv, 6)
                nc.vector.scalar_tensor_tensor(V[:, 1, :], V[:, 1, :], 0.25, V[:, 2, :], ALU.mult, ALU.add).then_inc(dv, 1)
                v.wait_ge(pl, 1)
                nc.vector.tensor_scalar(V[:, 2, :], V[:, 3, :], XS, None, ALU.mult).then_inc(dv, 1)
                v.wait_ge(dv, 8)
            with v.Fori(0, GROUPS) as i:
                for u in range(U):
                    j = i * U + u
                    v.wait_ge(up, j + 1)
                    if nodes:
                        v.wait_ge(kept, j + 1)
                    if source == "norm":
                        nc.vector.tensor_scalar(c.R[:, u, :], c.rows(c.X, j), V[:, 0, ds(j, 1)], V[:, 2, ds(j, 1)], ALU.subtract, ALU.mult).then_inc(row, 1)
                    else:
                        nc.vector.tensor_scalar(c.R[:, u, :], c.rows(c.G, j), c.SCL[:, 0:1], None, ALU.mult).then_inc(row, 1)
                for u in range(U):
                    j = i * U + u
                    v.wait_ge(hi, j + 1)
                    nc.vector.tensor_tensor(c.cols(dst_l, j), c.PS[:, u, 0:D].rearrange("p (k n) -> p k n", k=KB), c.cols(dst_h, j), ALU.subtract).then_inc(lo, 1)

        @block.gpsimd
        def _(g):
            if source == "norm":
                g.wait_ge(dv, 7)
                nc.gpsimd.tensor_tensor(V[:, 3, :], V[:, 1, :], c.EPSP[:], ALU.pow).then_inc(pl, 1)
            if nodes:
                g.sem_inc(kept, U)
                with g.Fori(0, GROUPS) as i:
                    for u in range(U):
                        j = i * U + u
                        g.wait_ge(row, j + 1)
                        nc.gpsimd.tensor_copy(c.HL[:, ds(j * 2 * D, D)], c.R[:, u, :]).then_inc(kept_hi, 1)
                        g.wait_ge(kept_hi, j + 1)
                        nc.gpsimd.tensor_tensor(c.HL[:, ds(j * 2 * D + D, D)], c.R[:, u, :], c.HL[:, ds(j * 2 * D, D)], ALU.subtract).then_inc(kept, 1)

        @block.tensor
        def _(t):
            t.sem_inc(up, U)
            with t.Fori(0, GROUPS) as i:
                for u in range(U):
                    j = i * U + u
                    t.wait_ge(row, j + 1)
                    t.wait_ge(lo, j + 1)
                    nc.tensor.transpose(c.PS[:, u, 0:P], c.R[:, u, 0:P], c.ident[:])
                    nc.tensor.transpose(c.PS[:, u, P:D], c.R[:, u, P:D], c.ident[:]).then_inc(up, 1)

        @block.scalar
        def _(a):
            with a.Fori(0, GROUPS) as i:
                for u in range(U):
                    j = i * U + u
                    a.wait_ge(up, j + 1 + U)
                    nc.scalar.copy(c.cols(dst_h, j), c.PS[:, u, 0:D].rearrange("p (k n) -> p k n", k=KB)).then_inc(hi, 1)


def aggregate(c, tag, kind):
    nc = c.nc
    arrived = [c.sem(f"{tag}_block{u}") for u in range(U)]
    summed, low, row = c.sem(f"{tag}_summed"), c.sem(f"{tag}_low"), c.sem(f"{tag}_row")
    up, hi, lo = c.sem(f"{tag}_turned"), c.sem(f"{tag}_hi"), c.sem(f"{tag}_lo")
    used = c.sem(f"{tag}_row_used")
    looped = c.sem(f"{tag}_looped")
    biased = c.sem(f"{tag}_biased")
    conv = kind in ("conv", "last")

    with nc.Block() as block:
        def turn_tile(t, i, u):
            j = i * U + u
            t.wait_ge(row, j + 1 + U)
            t.wait_ge(lo, j + 1)
            bank = 5 + u % 3
            nc.tensor.transpose(c.PS[:, bank, 0:P], c.R[:, u, 0:P], c.ident[:])
            nc.tensor.transpose(c.PS[:, bank, P:D], c.R[:, u, P:D], c.ident[:]).then_inc(up, 1)

        def copy_hi(a, i, u):
            j = i * U + u
            a.wait_ge(up, j + 2)
            nc.scalar.copy(c.cols(c.MTh, j), c.PS[:, 5 + u % 3, 0:D].rearrange("p (k n) -> p k n", k=KB)).then_inc(hi, 1)

        def low_part(v, i, u):
            j = i * U + u
            v.wait_ge(hi, j + 1)
            nc.vector.tensor_tensor(c.cols(c.MTl, j), c.PS[:, 5 + u % 3, 0:D].rearrange("p (k n) -> p k n", k=KB), c.cols(c.MTh, j), ALU.subtract).then_inc(lo, 1)

        @block.sync
        def _(sp):
            for u in range(U):
                sp.dma_start(c.ATB[:, u * ATCOLS:(u + 1) * ATCOLS], c.dram["adj"][u]).then_inc(arrived[u], 16)
            with sp.Fori(1, GROUPS) as i:
                for u in range(U):
                    row, multiplied = sp.snap((i * U + u) * P), sp.snap(i * U + (u - U + 1))
                    sp.wait_ge(summed, multiplied)
                    sp.dma_start(c.ATB[:, u * ATCOLS:(u + 1) * ATCOLS], c.dram["adj"].rearrange("a p n -> (a p) n")[ds(row, P)]).then_inc(arrived[u], 16)

        @block.tensor
        def _(t):
            if kind == "mean":
                t.sem_inc(up, 1)
            with t.Fori(0, GROUPS) as i:
                for u in range(U):
                    j = i * U + u
                    t.wait_ge(arrived[u], i * 16 + 16)
                    t.wait_ge(row, j + 1)
                    for s in range(TILES):
                        m = nc.tensor.matmul(c.PS[:, u, :], c.ATB[:, u * ATCOLS + s * P:u * ATCOLS + (s + 1) * P],
                                             c.HL[:, s * 2 * D:(s + 1) * 2 * D], start=(s == 0), stop=(s == TILES - 1))
                    m.then_inc(summed, 1)
                    if kind == "mean" and u > 0:
                        turn_tile(t, i, u - 1)
                if kind == "mean":
                    turn_tile(t, i, U - 1)

        @block.scalar
        def _(a):
            with a.Fori(0, GROUPS) as i:
                for u in range(U):
                    j = i * U + u
                    a.wait_ge(summed, j + 1)
                    a.wait_ge(row, j + 1)
                    nc.scalar.mul(c.TMP[:, u, :], c.PS[:, u, D:2 * D], c.SCL[:, ds(j, 1)]).then_inc(low, 1)
                    if kind == "mean" and u > 0:
                        copy_hi(a, i, u - 1)
                if kind == "mean":
                    copy_hi(a, i, U - 1)

        @block.vector
        def _(v):
            v.sem_inc(row, U)
            if kind == "mean":
                v.sem_inc(lo, 2)
            if conv:
                v.sem_inc(used, U)
            with v.Fori(0, GROUPS) as i:
                for u in range(U):
                    j = i * U + u
                    v.wait_ge(low, j + 1)
                    if kind == "mean":
                        v.wait_ge(up, i * U + 1)
                    else:
                        v.wait_ge(used, j + 1)
                    nc.vector.scalar_tensor_tensor(c.R[:, u, :], c.PS[:, u, 0:D], c.SCL[:, ds(j, 1)], c.TMP[:, u, :], ALU.mult, ALU.add).then_inc(row, 1)
                    if conv:
                        v.wait_ge(row, j + 1 + U)
                        nc.vector.scalar_tensor_tensor(c.R[:, u, :], c.rows(c.G, j), c.DINV[:, ds(j, 1)], c.R[:, u, :], ALU.mult, ALU.add).then_inc(looped, 1)
                    if kind == "mean" and u > 0:
                        low_part(v, i, u - 1)
                if kind == "mean":
                    low_part(v, i, U - 1)
                if conv:
                    for u in range(U):
                        j = i * U + u
                        v.wait_ge(biased, j + 1)
                        if kind == "conv":
                            nc.vector.tensor_scalar(c.rows(c.G, j), c.R[:, u, :], 0.0, None, ALU.max).then_inc(used, 1)
                        else:
                            nc.vector.scalar_tensor_tensor(c.rows(c.X, j), c.R[:, u, :], 0.0, c.rows(c.X, j), ALU.max, ALU.add).then_inc(used, 1)

        @block.gpsimd
        def _(g):
            if kind == "mean":
                return
            if kind == "residual":
                g.sem_inc(used, U)
            with g.Fori(0, GROUPS) as i:
                for u in range(U):
                    j = i * U + u
                    if kind == "residual":
                        g.wait_ge(row, j + 1 + U)
                        nc.gpsimd.tensor_tensor(c.rows(c.X, j), c.rows(c.X, j), c.R[:, u, :], ALU.add).then_inc(used, 1)
                    else:
                        g.wait_ge(looped, j + 1)
                        nc.gpsimd.tensor_tensor(c.R[:, u, :], c.R[:, u, :], c.ROWB[:, 1 if kind == "conv" else 2, :], ALU.add).then_inc(biased, 1)


def pairs(wh, wl, xh, xl):
    return ((wh, xh), (wh, xl), (wl, xh))


def dense(c, tag, hb_count, operands, w, w2, w2_cols, act_scale, bias0, hid_scale, evac):
    nc = c.nc
    HT = c.HL[:].rearrange("p (a n) -> p a n", n=CHUNK)
    full, act, split = c.sem(f"{tag}_hidden"), c.sem(f"{tag}_relu"), c.sem(f"{tag}_split")
    out_full, out_free = c.sem(f"{tag}_out"), c.sem(f"{tag}_out_copied")
    split_hi = c.sem(f"{tag}_split_hi")
    ow = w2_cols

    def ht(i, part, hb, u):
        return c.HL[:, ds(((i & 1) * 8 + part * 4 + hb) * CHUNK + u * P, P)]

    with nc.Block() as block:
        @block.tensor
        def _(t):
            def first(i):
                for hb in range(hb_count):
                    t.wait_ge(act, i * hb_count + hb + 1)
                    for half in range(2):
                        out = c.PS[:, 2 * (hb % 2) + half, 0:HALF]
                        todo = []
                        for w0, xh, xl in operands:
                            for kb in range(KB):
                                a = w0 + kb * hb_count * P + hb * P
                                for wp, x in ((0, xh), (0, xl), (1, xh)):
                                    todo.append((w[:, wp, a:a + P], x[:, ds(i * CHUNK + (kb * NP + half * HALF), HALF)]))
                        for n, (l, r) in enumerate(todo):
                            m = nc.tensor.matmul(out, l, r, start=(n == 0), stop=(n == len(todo) - 1))
                    m.then_inc(full, 1)

            def second(i):
                t.wait_ge(split, i * hb_count + hb_count + 2)
                for u in range(U):
                    t.wait_ge(out_free, i * U + u + 1)
                    out = c.PS[:, 4 + u % 3, 0:ow]
                    n = 0
                    for hb in range(hb_count):
                        for hp, wp in ((0, 0), (1, 0), (0, 1)):
                            a = w2 + hb * ow
                            m = nc.tensor.matmul(out, ht(i, hp, hb, u), w[:, wp, a:a + ow], start=(n == 0), stop=(n == 3 * hb_count - 1))
                            n += 1
                    m.then_inc(out_full, 1)

            first(0)
            with t.Fori(1, GROUPS) as i:
                first(i)
                second(i - 1)
            second(GROUPS - 1)

        @block.scalar
        def _(a):
            a.sem_inc(act, 2)
            with a.Fori(0, GROUPS) as i:
                for hb in range(hb_count):
                    a.wait_ge(full, i * hb_count + hb + 1)
                    a.wait_ge(split, i * hb_count + hb + 1)
                    nc.scalar.activation(c.HF[:, hb % 2, :].rearrange("p (a n) -> p a n", a=2), c.PS[:, 2 * (hb % 2):2 * (hb % 2) + 2, 0:HALF], ACT.Relu,
                                         bias=c.COLB[:, bias0 + hb:bias0 + hb + 1], scale=act_scale).then_inc(act, 1)

        @block.vector
        def _(v):
            v.sem_inc(split, 2)
            v.sem_inc(out_free, 2)

            def splits(i):
                for hb in range(hb_count):
                    v.wait_ge(act, i * hb_count + hb + 3)
                    h = c.HL[:, ds(((i & 1) * 8 + hb) * CHUNK, CHUNK)]
                    l = c.HL[:, ds(((i & 1) * 8 + 4 + hb) * CHUNK, CHUNK)]
                    nc.vector.tensor_scalar(h, c.HF[:, hb % 2, :], hid_scale, None, ALU.mult).then_inc(split_hi, 1)
                    v.wait_ge(split_hi, i * hb_count + hb + 1)
                    nc.vector.scalar_tensor_tensor(l, c.HF[:, hb % 2, :], hid_scale, h, ALU.mult, ALU.subtract).then_inc(split, 1)

            def outs(i):
                for u in range(U):
                    v.wait_ge(out_full, i * U + u + 1)
                    evac(nc.vector, i * U + u, c.PS[:, 4 + u % 3, 0:ow]).then_inc(out_free, 1)

            splits(0)
            with v.Fori(1, GROUPS) as i:
                splits(i)
                outs(i - 1)
            outs(GROUPS - 1)


def scale_rows(c, tag, factors, split):
    nc = c.nc
    dv, pl = c.sem(f"{tag}_steps"), c.sem(f"{tag}_max")
    with nc.Block() as block:
        @block.vector
        def _(v):
            nc.vector.tensor_reduce(c.MX[:, 11:12], c.G[:], AX.X, ALU.max, apply_absolute_value=True).then_inc(dv, 1)
            v.wait_ge(pl, 1)
            nc.vector.tensor_scalar(c.MX[:, 11:12], c.MXR[:, 11:12], 1e-30, None, ALU.max).then_inc(dv, 1)
            v.wait_ge(dv, 2)
            nc.vector.tensor_scalar(c.SIG[:, 11:12].bitcast(I32), c.MX[:, 11:12].bitcast(I32), EXPO, EXPO, ALU.bitwise_and, ALU.bitwise_xor).then_inc(dv, 1)
            nc.vector.tensor_scalar(c.PK[:, 11:12].bitcast(I32), c.MX[:, 11:12].bitcast(I32), EXPO, None, ALU.bitwise_and).then_inc(dv, 1)
            v.wait_ge(dv, 4)
            if split:
                nc.vector.tensor_scalar(c.SIG[:, 11:12], c.SIG[:, 11:12], 8192.0, None, ALU.mult).then_inc(dv, 1)
                nc.vector.tensor_scalar(c.SCL[:], factors[:], c.PK[:, 11:12], 2.0 ** -14, ALU.mult, ALU.mult).then_inc(dv, 1)
                v.wait_ge(dv, 5)
                hl = c.HL[:].rearrange("p (t d) -> p t d", d=2 * D)
                g3 = c.G[:].rearrange("p (t d) -> p t d", d=D)
                nc.vector.tensor_scalar(hl[:, :, 0:D], g3, c.SIG[:, 11:12], None, ALU.mult).then_inc(dv, 1)
                v.wait_ge(dv, 7)
                nc.vector.scalar_tensor_tensor(hl[:, :, D:2 * D], g3, c.SIG[:, 11:12], hl[:, :, 0:D], ALU.mult, ALU.subtract).then_inc(dv, 1)
            else:
                nc.vector.tensor_scalar(c.SCL[:, 0:1], c.SIG[:, 11:12], 8192.0, None, ALU.mult).then_inc(dv, 1)
                nc.vector.tensor_scalar(c.SCL[:, 1:2], c.PK[:, 11:12], 2.0 ** -14, None, ALU.mult).then_inc(dv, 1)

        @block.gpsimd
        def _(g):
            g.wait_ge(dv, 1)
            nc.gpsimd.partition_all_reduce(c.MXR[:, 11:12], c.MX[:, 11:12], P, ABSMAX).then_inc(pl, 1)


def small_ops(c, tag, ops):
    nc = c.nc
    dv = c.sem(f"{tag}_steps")
    with nc.Block() as block:
        @block.vector
        def _(v):
            for n, op in enumerate(ops):
                if n:
                    v.wait_ge(dv, n)
                op(nc.vector).then_inc(dv, 1)


def project(c, tag, w0, factor):
    nc = c.nc
    full, free = c.sem(f"{tag}_out"), c.sem(f"{tag}_copied")
    with nc.Block() as block:
        @block.tensor
        def _(t):
            with t.Fori(0, GROUPS) as i:
                for u in range(U):
                    j = i * U + u
                    t.wait_ge(free, j + 1)
                    n = 0
                    for kb in range(KB):
                        for x, wp in ((c.XTh, 0), (c.XTl, 0), (c.XTh, 1)):
                            m = nc.tensor.matmul(c.PS[:, u, 0:D], x[:, ds(j * P + kb * NP, P)], c.G1W[:, wp, w0 + kb * D:w0 + (kb + 1) * D],
                                                 start=(n == 0), stop=(n == 3 * KB - 1))
                            n += 1
                    m.then_inc(full, 1)

        @block.scalar
        def _(a):
            a.sem_inc(free, U)
            with a.Fori(0, GROUPS) as i:
                for u in range(U):
                    j = i * U + u
                    a.wait_ge(full, j + 1)
                    nc.scalar.mul(c.rows(c.G, j), c.PS[:, u, 0:D], factor[:, ds(j, 1)]).then_inc(free, 1)


def experts(c, tag, layer, softmax):
    nc = c.nc
    stage = c.ATB[:].bitcast(F32)
    STG = stage[:, 0:4096]
    W = c.ATB[:, 8192:16384]
    HT = c.G[:].bitcast(F16)
    S, CW, CMP, RANK, MEX, CWK = c.SG, c.CW, c.CMP, c.RANK, c.MEX, c.CWK
    CWT, CWR, EK, EM, EMR = c.CWT, c.CWR, c.EK, c.EM, c.EMR
    PS = c.PS
    gate_full, gv, ga = c.sem(f"{tag}_gates"), c.sem(f"{tag}_gate_steps"), c.sem(f"{tag}_exp")
    cw_row, cw_up, cw_in, b2_full, b2_free = (c.sem(f"{tag}_{x}") for x in ("cw_row", "cw_turned", "cw_copied", "b2_out", "b2_added"))
    staged = [c.sem(f"{tag}_staged{s}") for s in range(2)]
    mx, mxr, bits, wsplit, whi = (c.sem(f"{tag}_{x}") for x in ("max", "max_all", "scales", "weights", "weights_hi"))
    full, act, split, split_hi = (c.sem(f"{tag}_{x}") for x in ("hidden", "gelu", "split", "split_hi"))
    out_full, out_free = c.sem(f"{tag}_out"), c.sem(f"{tag}_out_added")
    gw = 1536 + layer * KB * E

    with nc.Block() as block:
        @block.sync
        def _(sp):
            for e in range(2):
                sp.dma_start(STG[:, e * 2048:(e + 1) * 2048], c.dram[f"ffn_w{layer}"][e]).then_inc(staged[e], 16)
            with sp.Fori(1, E // 2) as i:
                for s in range(2):
                    row, used = sp.snap((i * 2 + s) * P), sp.snap(i * 2 + (s - 1))
                    sp.wait_ge(wsplit, used)
                    sp.dma_start(STG[:, s * 2048:(s + 1) * 2048], c.dram[f"ffn_w{layer}"].rearrange("a p n -> (a p) n")[ds(row, P)]).then_inc(staged[s], 16)

        @block.gpsimd
        def _(g):
            for e in range(E):
                g.wait_ge(mx, 3 * e + 3)
                nc.gpsimd.partition_all_reduce(EMR[:], EM[:], P, ABSMAX).then_inc(mxr, 1)

        @block.tensor
        def _(t):
            with t.Fori(0, TILES) as j:
                n = 0
                for kb in range(KB):
                    for x, wp in ((c.XTh, 0), (c.XTl, 0), (c.XTh, 1)):
                        m = nc.tensor.matmul(PS[:, 7, ds(j * E, E)], x[:, ds(j * P + kb * NP, P)], c.G1W[:, wp, gw + kb * E:gw + (kb + 1) * E],
                                             start=(n == 0), stop=(n == 3 * KB - 1))
                        n += 1
                m.then_inc(gate_full, 1)
            t.sem_inc(cw_up, U)
            with t.Fori(0, GROUPS) as i:
                for u in range(U):
                    j = i * U + u
                    t.wait_ge(cw_row, j + 1)
                    t.wait_ge(cw_in, j + 1)
                    nc.tensor.transpose(PS[0:E, 6, 0:P], CWR[:, u, :], c.ident[:]).then_inc(cw_up, 1)
                    t.wait_ge(cw_in, j + 2)
                    t.wait_ge(b2_free, j + 1)
                    nc.tensor.matmul(PS[:, u % 3, 0:D], CWT[:, u, :], c.FB2[:, layer, :], start=True, stop=True).then_inc(b2_full, 1)

            def first(n, e, ch):
                t.wait_ge(wsplit, e + 1)
                for hb in range(HB):
                    t.wait_ge(act, n * HB + hb + 1)
                    for half in range(2):
                        k = 0
                        for kb in range(KB):
                            for wp, x in ((0, c.XTh), (0, c.XTl), (1, c.XTh)):
                                m = nc.tensor.matmul(PS[:, 2 * (hb % 2) + half, 0:HALF], W[:, ds((e & 1) * 4096 + (wp * 2048 + kb * HID + hb * P), P)],
                                                     x[:, ds(ch * CHUNK + (kb * NP + half * HALF), HALF)], start=(k == 0), stop=(k == 3 * KB - 1))
                                k += 1
                    m.then_inc(full, 1)

            def second(n, e):
                t.wait_ge(split, n * HB + HB + 2)
                for u in range(U):
                    t.wait_ge(out_free, n * U + u + 1)
                    k = 0
                    for hb in range(HB):
                        for hp, wp in ((0, 0), (1, 0), (0, 1)):
                            m = nc.tensor.matmul(PS[:, 4 + u % 3, 0:D], HT[:, ds((n & 1) * 8 * CHUNK + ((hp * 4 + hb) * CHUNK + u * P), P)],
                                                 W[:, ds((e & 1) * 4096 + (wp * 2048 + 1024 + hb * D), D)], start=(k == 0), stop=(k == 3 * HB - 1))
                            k += 1
                    m.then_inc(out_full, 1)

            t.wait_ge(b2_free, TILES + 2)
            first(0, 0, 0)
            with t.Fori(1, E * GROUPS) as n:
                first(n, t.snap(n // GROUPS), t.snap(n % GROUPS))
                second(n - 1, t.snap((n - 1) // GROUPS))
            second(E * GROUPS - 1, E - 1)

        @block.scalar
        def _(a):
            if softmax:
                a.wait_ge(gv, 4)
                nc.scalar.activation(S[:], S[:], ACT.Exp).then_inc(ga, 1)
            a.sem_inc(act, 2)
            a.sem_inc(cw_in, 1)
            with a.Fori(0, GROUPS) as i:
                for u in range(U):
                    j = i * U + u
                    a.wait_ge(cw_up, j + 1 + U)
                    nc.scalar.copy(CWT[:, u, :], PS[0:E, 6, 0:P]).then_inc(cw_in, 1)
            nc.scalar.preload_act_table(ACT.Gelu)
            with a.Fori(0, E) as e:
                a.wait_ge(bits, e * 2 + 2)
                with a.Fori(0, GROUPS) as ch:
                    n = e * GROUPS + ch
                    for hb in range(HB):
                        a.wait_ge(full, n * HB + hb + 1)
                        a.wait_ge(split, n * HB + hb + 1)
                        nc.scalar.activation(c.HF[:, hb % 2, :].rearrange("p (a n) -> p a n", a=2), PS[:, 2 * (hb % 2):2 * (hb % 2) + 2, 0:HALF], ACT.Gelu,
                                             bias=c.FB1[:, layer, ds(e * HB + hb, 1)], scale=EK[:, 0, ds(e, 1)]).then_inc(act, 1)

        @block.vector
        def _(v):
            n = [0]

            def step(ins):
                n[0] += 1
                ins.then_inc(gv, 1)
                v.wait_ge(gv, n[0])

            v.wait_ge(gate_full, TILES)
            s3 = S[:].rearrange("p (t e) -> p t e", e=E)
            bias = c.GATEB[:, layer, :].unsqueeze(1).to_broadcast([P, TILES, E])
            step(nc.vector.tensor_scalar(S[:], PS[:, 7, 0:TILES * E], c.PK[:, 5 + layer:6 + layer], 2.0 ** -18, ALU.mult, ALU.mult))
            step(nc.vector.tensor_tensor(s3, s3, bias, ALU.add))
            if softmax:
                step(nc.vector.tensor_reduce(MEX[:], s3, AX.X, ALU.max))
                step(nc.vector.tensor_tensor(s3, s3, MEX[:].unsqueeze(2).to_broadcast([P, TILES, E]), ALU.subtract))
                v.wait_ge(ga, 1)
                step(nc.vector.tensor_reduce(MEX[:], s3, AX.X, ALU.add))
                step(nc.vector.reciprocal(MEX[:], MEX[:]))
                step(nc.vector.tensor_tensor(s3, s3, MEX[:].unsqueeze(2).to_broadcast([P, TILES, E]), ALU.mult))
            cmp4 = CMP[:, 0, :].rearrange("p (t a b) -> p t a b", a=E, b=E)
            eq4 = CMP[:, 1, :].rearrange("p (t a b) -> p t a b", a=E, b=E)
            other = s3.unsqueeze(2).to_broadcast([P, TILES, E, E])
            own = s3.unsqueeze(3).to_broadcast([P, TILES, E, E])
            low = c.ELOW[:].rearrange("p (a b) -> p a b", b=E).unsqueeze(1).to_broadcast([P, TILES, E, E])
            step(nc.vector.tensor_tensor(cmp4, other, own, ALU.is_gt))
            step(nc.vector.tensor_tensor(eq4, other, own, ALU.is_equal))
            step(nc.vector.tensor_tensor(eq4, eq4, low, ALU.mult))
            step(nc.vector.tensor_tensor(CMP[:, 0, :], CMP[:, 0, :], CMP[:, 1, :], ALU.add))
            step(nc.vector.tensor_reduce(RANK[:], CMP[:, 0, :].rearrange("p (t b) -> p t b", b=E), AX.X, ALU.add))
            step(nc.vector.tensor_scalar(CW[:], RANK[:], 2.0, None, ALU.is_lt))
            if softmax:
                step(nc.vector.tensor_tensor(CW[:], CW[:], S[:], ALU.mult))
            v.sem_inc(b2_free, 2)
            v.sem_inc(split, 2)
            v.sem_inc(out_free, 2)
            with v.Fori(0, GROUPS) as i:
                for u in range(U):
                    v.wait_ge(cw_up, i * U + u + 1)
                    nc.vector.tensor_copy(CWR[:, u, :], CW[:, ds(i * U * E + u * E, E)]).then_inc(cw_row, 1)
                for u in range(U):
                    j = i * U + u
                    v.wait_ge(b2_full, j + 1)
                    nc.vector.tensor_tensor(c.rows(c.X, j), PS[:, u % 3, 0:D], c.rows(c.X, j), ALU.add).then_inc(b2_free, 1)

            def maxima(e, s, turn_no):
                v.wait_ge(staged[s], turn_no * 16 + 16)
                nc.vector.tensor_reduce(EM[:, 0:2], STG[:, s * 2048:(s + 1) * 2048].rearrange("p (a n) -> p a n", a=2), AX.X, ALU.max, apply_absolute_value=True).then_inc(mx, 1)
                nc.vector.tensor_reduce(EM[:, 2:3], c.FB1[:, layer, ds(e * HB, HB)], AX.X, ALU.max, apply_absolute_value=True).then_inc(mx, 2)

            def scales(e, s):
                v.wait_ge(mxr, e + 1)
                q = lambda k: es_base(e) + k
                nc.vector.tensor_scalar(EM[:, 0:2], EMR[:, 0:2], 1e-30, None, ALU.max).then_inc(es, 1)
                nc.vector.scalar_tensor_tensor(EM[:, 2:3], EMR[:, 0:1], 256.0, EMR[:, 2:3], ALU.mult, ALU.add).then_inc(es, 1)
                v.wait_ge(es, q(2))
                nc.vector.tensor_scalar(EM[:, 2:3], EM[:, 2:3], 1e-30, None, ALU.max).then_inc(es, 1)
                v.wait_ge(es, q(3))
                nc.vector.tensor_scalar(c.ESIG[:].bitcast(I32), EM[:].bitcast(I32), EXPO, EXPO, ALU.bitwise_and, ALU.bitwise_xor).then_inc(es, 1)
                nc.vector.tensor_scalar(c.EPK[:].bitcast(I32), EM[:].bitcast(I32), EXPO, None, ALU.bitwise_and).then_inc(es, 1)
                v.wait_ge(es, q(5))
                nc.vector.tensor_scalar(EK[:, 0, ds(e, 1)], c.EPK[:, 0:1], 2.0 ** -18, None, ALU.mult).then_inc(bits, 1)
                nc.vector.tensor_scalar(EK[:, 1, ds(e, 1)], c.ESIG[:, 2:3], 2.0 ** 13, None, ALU.mult).then_inc(bits, 1)
                nc.vector.tensor_scalar(EK[:, 2, ds(e, 1)], c.EPK[:, 1:2], c.EPK[:, 2:3], 2.0 ** -24, ALU.mult, ALU.mult).then_inc(es, 1)
                nc.vector.tensor_scalar(c.ESIG[:, 0:2], c.ESIG[:, 0:2], 512.0, None, ALU.mult).then_inc(es, 1)
                v.wait_ge(es, q(7))
                nc.vector.tensor_scalar(CWK[:, ds(e * TILES, TILES)], CW[:].rearrange("p (t e) -> p e t", e=E)[:, ds(e, 1), :].rearrange("p a t -> p (a t)"),
                                        EK[:, 2, ds(e, 1)], None, ALU.mult).then_inc(es, 1)
                for k in range(2):
                    nc.vector.tensor_scalar(W[:, s * 4096 + k * 1024:s * 4096 + (k + 1) * 1024], STG[:, s * 2048 + k * 1024:s * 2048 + (k + 1) * 1024],
                                            c.ESIG[:, k:k + 1], None, ALU.mult).then_inc(es, 1)
                v.wait_ge(es, q(10))
                nc.vector.scalar_tensor_tensor(W[:, s * 4096 + 2048:s * 4096 + 3072], STG[:, s * 2048:s * 2048 + 1024], c.ESIG[:, 0:1],
                                               W[:, s * 4096:s * 4096 + 1024], ALU.mult, ALU.subtract).then_inc(es, 1)
                nc.vector.scalar_tensor_tensor(W[:, s * 4096 + 3072:s * 4096 + 4096], STG[:, s * 2048 + 1024:s * 2048 + 2048], c.ESIG[:, 1:2],
                                               W[:, s * 4096 + 1024:s * 4096 + 2048], ALU.mult, ALU.subtract).then_inc(wsplit, 1)

            es = c.sem(f"{tag}_expert_steps")

            def es_base(e):
                return e * 11

            def splits(m, e):
                for hb in range(HB):
                    v.wait_ge(act, m * HB + hb + 3)
                    h = HT[:, ds((m & 1) * 8 * CHUNK + hb * CHUNK, CHUNK)]
                    l = HT[:, ds((m & 1) * 8 * CHUNK + (4 + hb) * CHUNK, CHUNK)]
                    nc.vector.tensor_scalar(h, c.HF[:, hb % 2, :], EK[:, 1, ds(e, 1)], None, ALU.mult).then_inc(split_hi, 1)
                    v.wait_ge(split_hi, m * HB + hb + 1)
                    nc.vector.scalar_tensor_tensor(l, c.HF[:, hb % 2, :], EK[:, 1, ds(e, 1)], h, ALU.mult, ALU.subtract).then_inc(split, 1)

            def outs(m, ch):
                for u in range(U):
                    v.wait_ge(out_full, m * U + u + 1)
                    x = c.X[:, ds(ch * (U * D) + u * D, D)]
                    nc.vector.scalar_tensor_tensor(x, PS[:, 4 + u % 3, 0:D], CWK[:, ds(m * U + u, 1)], x, ALU.mult, ALU.add).then_inc(out_free, 1)

            def expert(e, s, more, turn_no, lead):
                if more:
                    maxima(e + 1, 1 - s, turn_no)
                splits(e * GROUPS, e)
                if lead:
                    outs(e * GROUPS - 1, GROUPS - 1)
                if more:
                    scales(e + 1, 1 - s)
                with v.Fori(1, GROUPS) as ch:
                    splits(e * GROUPS + ch, e)
                    outs(e * GROUPS + ch - 1, ch - 1)

            maxima(0, 0, 0)
            scales(0, 0)
            expert(0, 0, True, 0, False)
            with v.Fori(0, E // 2 - 1) as h:
                expert(h * 2 + 1, 1, True, h + 1, True)
                expert(h * 2 + 2, 0, True, h + 1, True)
            expert(E - 1, 1, False, 0, True)
            outs(E * GROUPS - 1, GROUPS - 1)


def store_phase(c):
    nc = c.nc
    done = c.sem("out_stored")
    with nc.Block() as block:
        @block.sync
        def _(sp):
            full = (TILES - 1) * P
            x3 = c.X[:].rearrange("p (t d) -> p t d", d=D)
            sp.dma_start(c.dram["out"][0:full].rearrange("(t p) d -> p t d", p=P), x3[:, 0:TILES - 1, :]).then_inc(done, 16)
            sp.dma_start(c.dram["out"][full:], x3[0:TAIL, TILES - 1, :]).then_inc(done, 16)
            sp.wait_ge(done, 32)


def build_program(nc, dram):
    with ExitStack() as ctx:
        c = Core(nc, ctx, dram)
        mul, cols = ALU.mult, lambda t, k: t[:, k:k + 1]
        setup_phase(c)
        adjacency_phase(c)

        turn(c, "norm0", "norm", c.XTh, c.XTl, True)
        x3 = c.X[:].rearrange("p (t d) -> p t d", d=D)
        small_ops(c, "gnn0", [
            lambda v: v.tensor_copy(c.SCL[:], c.INV[:]),
            lambda v: v.tensor_scalar(cols(c.FAC, 0), cols(c.PK, 0), 2.0 ** -18, None, mul),
            lambda v: v.tensor_scalar(cols(c.FAC, 1), cols(c.PK, 9), cols(c.PK, 1), 2.0 ** -24, mul, mul),
            lambda v: v.tensor_tensor(x3, x3, c.ROWB[:, 0, :].unsqueeze(1).to_broadcast([P, TILES, D]), ALU.add),
        ])
        aggregate(c, "mean0", "mean")

        def sage_out(v, j, ps):
            v.tensor_scalar(c.rows(c.G, j), ps[:, 0:D], cols(c.FAC, 1), None, mul)
            return v.scalar_tensor_tensor(c.rows(c.X, j), ps[:, D:2 * D], cols(c.FAC, 1), c.rows(c.X, j), mul, ALU.add)

        dense(c, "sage", HB, [(0, c.MTh, c.MTl), (1024, c.XTh, c.XTl)], c.G0W, 2048, 2 * D, cols(c.FAC, 0), 0, cols(c.SIG, 9), sage_out)
        scale_rows(c, "scale0", c.INV, True)
        aggregate(c, "mean1", "residual")

        turn(c, "norm1", "norm", c.XTh, c.XTl, False)
        experts(c, "moe0", 0, False)
        c.clear_semaphores()

        turn(c, "norm2", "norm", c.XTh, c.XTl, False)
        small_ops(c, "gnn1", [
            lambda v: v.tensor_scalar(cols(c.FAC, 0), cols(c.PK, 2), 2.0 ** -18, None, mul),
            lambda v: v.tensor_scalar(cols(c.FAC, 1), cols(c.PK, 10), cols(c.PK, 3), 2.0 ** -24, mul, mul),
            lambda v: v.tensor_scalar(c.FAC[:, 2:], c.DINV[:], cols(c.FAC, 1), None, mul),
        ])

        def conv_out(v, j, ps):
            return v.tensor_scalar(c.rows(c.G, j), ps, c.FAC[:, ds(j + 2, 1)], None, mul)

        dense(c, "conv0", KB, [(0, c.XTh, c.XTl)], c.G1W, 512, D, cols(c.FAC, 0), HB, cols(c.SIG, 10), conv_out)
        scale_rows(c, "scale1", c.DINV, True)
        aggregate(c, "hop0", "conv")
        scale_rows(c, "scale2", None, False)
        small_ops(c, "gnn2", [
            lambda v: v.tensor_scalar(cols(c.FAC, 0), cols(c.PK, 4), cols(c.SCL, 1), 2.0 ** -10, mul, mul),
            lambda v: v.tensor_scalar(c.FAC[:, 2:], c.DINV[:], cols(c.FAC, 0), None, mul),
        ])
        turn(c, "rows1", "scaled", c.XTh, c.XTl, False)
        project(c, "conv1", 1024, c.FAC[:, 2:])
        scale_rows(c, "scale3", c.DINV, True)
        aggregate(c, "hop1", "last")

        turn(c, "norm3", "norm", c.XTh, c.XTl, False)
        experts(c, "moe1", 1, True)
        store_phase(c)
        c.clear_semaphores()


def kernel(x, src, dst, L0_gnn_W1l, L0_gnn_b1, L0_gnn_W1r, L0_gnn_W2l, L0_gnn_b2, L0_gnn_W2r, L0_ffn_Wg, L0_ffn_bg,
           L0_ffn_W1, L0_ffn_b1, L0_ffn_W2, L0_ffn_b2, L1_gnn_weight, L1_gnn_bias, L1_gnn_conv_w, L1_gnn_conv_b,
           L1_ffn_gate_w, L1_ffn_gate_b, L1_ffn_W1, L1_ffn_b1, L1_ffn_W2, L1_ffn_b2):
    import concourse.bacc as bacc
    from concourse.bass_utils import run_bass_kernel_spmd

    def blocks(w):
        w = np.asarray(w)
        return w.reshape(-1, P, w.shape[1]).transpose(1, 0, 2).reshape(P, -1)

    def column(b):
        return np.asarray(b).reshape(-1, P).T

    arrays = {
        "x": x, "src": src, "dst": dst,
        "gnn_w": np.concatenate([
            blocks(np.asarray(L0_gnn_W1l).T), blocks(np.asarray(L0_gnn_W1r).T),
            blocks(np.concatenate([np.asarray(L0_gnn_W2l).T, np.asarray(L0_gnn_W2r).T], axis=1)),
            blocks(L1_gnn_weight), blocks(L1_gnn_conv_w[0]), blocks(L1_gnn_conv_w[1]),
            blocks(L0_ffn_Wg), blocks(L1_ffn_gate_w)], axis=1),
        "col_bias": np.concatenate([column(L0_gnn_b1), column(L1_gnn_bias)], axis=1),
        "L0_gnn_b2": L0_gnn_b2, "conv_b0": L1_gnn_conv_b[0], "conv_b1": L1_gnn_conv_b[1],
        "L0_ffn_bg": L0_ffn_bg, "L1_ffn_gate_b": L1_ffn_gate_b,
        "ffn_b1": np.stack([column(L0_ffn_b1), column(L1_ffn_b1)], axis=1),
        "L0_ffn_b2": L0_ffn_b2, "L1_ffn_b2": L1_ffn_b2,
    }
    for layer, (w1, w2) in enumerate(((L0_ffn_W1, L0_ffn_W2), (L1_ffn_W1, L1_ffn_W2))):
        arrays[f"ffn_w{layer}"] = np.stack([np.concatenate([blocks(w1[e]), blocks(w2[e])], axis=1) for e in range(E)])
    arrays = {f"in_{k}": np.ascontiguousarray(a) for k, a in arrays.items()}

    nc = bacc.Bacc("TRN2", target_bir_lowering=False, num_devices=1)
    dram = {k[3:]: nc.dram_tensor(k, a.shape, mybir.dt.from_np(a.dtype), kind="ExternalInput").ap() for k, a in arrays.items()}
    dram["adj"] = nc.dram_tensor("adjacency", (TILES, P, ATCOLS), F16).ap()
    dram["meta"] = nc.dram_tensor("window_ranges", (2 * P,), I32).ap()
    dram["out"] = nc.dram_tensor("out", (N_NODES, D), F32, kind="ExternalOutput").ap()
    build_program(nc, dram)
    r = run_bass_kernel_spmd(nc, [arrays], core_ids=[0])
    return r.results[0]["out"]
```
